# Optimizing a Trainium2 kernel written in Bass

```python
import numpy as np
import jax
import jax.numpy as jnp

def _softmax(x, axis=-1):
    return jax.nn.softmax(x, axis=axis)

def _gelu(x):
    return jax.nn.gelu(x, approximate=True)

def _silu(x):
    return jax.nn.silu(x)

def _sigmoid(x):
    return jax.nn.sigmoid(x)

def _layernorm(x, axis=-1, eps=1e-05):
    m = jnp.mean(x, axis=axis, keepdims=True)
    v = jnp.var(x, axis=axis, keepdims=True)
    return (x - m) / jnp.sqrt(v + eps)

def _scatter_add(tgt, idx, src, axis=0):
    return tgt.at[idx].add(src)

def _segment_sum(src, seg, n):
    return jax.ops.segment_sum(src, seg, n)
kernel_name = 'mk_rec_standalone_d1_rec_r8_518ced'

def setup_inputs(seed: int=0):
    np.random.seed(seed)
    _w = jnp.asarray

    def _rec_inputs():
        import jax
        import jax.numpy as jnp
        _rk = jax.random.key(seed)
        r_x = jax.random.randint(jax.random.fold_in(_rk, 1), (2048, 26, 8), 0, 125000, jnp.int32)
        return r_x
    r_x = _rec_inputs()

    def _L0_rec_setup():
        import jax, jax.numpy as jnp
        import numpy as np
        V = 125000
        D = 64
        F = 26
        L = 8
        B = 512
        IN_DIM = F * D
        HIDDENS = (1024, 1024, 512)
        key = jax.random.key(seed)
        ks = jax.random.split(key, 4 + 4 * len(HIDDENS))
        inp = {}
        inp['x'] = jax.random.randint(ks[0], (B, F, L), 0, V, dtype=jnp.int64)
        inp['emb_table'] = jax.random.normal(ks[1], (V, D), dtype=jnp.float32) * 0.01
        ki = 2
        for i, h in enumerate(HIDDENS):
            inp[f'w1_{i}'] = jax.random.normal(ks[ki], (IN_DIM, h), dtype=jnp.float32) * 0.02
            inp[f'b1_{i}'] = jnp.zeros((h,), dtype=jnp.float32)
            inp[f'w2_{i}'] = jax.random.normal(ks[ki + 1], (h, IN_DIM), dtype=jnp.float32) * 0.02
            inp[f'b2_{i}'] = jnp.zeros((IN_DIM,), dtype=jnp.float32)
            ki += 2
        inp['lin_w'] = jax.random.normal(ks[ki], (IN_DIM, 1), dtype=jnp.float32) * 0.02
        inp['lin_b'] = jnp.zeros((1,), dtype=jnp.float32)
        return inp
    _L0_rec_all = _L0_rec_setup()
    _L0_rec_in = {k: v for k, v in _L0_rec_all.items() if k in ('emb_table', 'w1_0', 'b1_0', 'w2_0', 'b2_0', 'w1_1', 'b1_1', 'w2_1', 'b2_1', 'w1_2', 'b1_2', 'w2_2', 'b2_2', 'lin_w', 'lin_b')}
    del _L0_rec_all
    return {'r_x': r_x, 'L0_rec_emb_table': _L0_rec_in['emb_table'], 'L0_rec_w1_0': _L0_rec_in['w1_0'], 'L0_rec_b1_0': _L0_rec_in['b1_0'], 'L0_rec_w2_0': _L0_rec_in['w2_0'], 'L0_rec_b2_0': _L0_rec_in['b2_0'], 'L0_rec_w1_1': _L0_rec_in['w1_1'], 'L0_rec_b1_1': _L0_rec_in['b1_1'], 'L0_rec_w2_1': _L0_rec_in['w2_1'], 'L0_rec_b2_1': _L0_rec_in['b2_1'], 'L0_rec_w1_2': _L0_rec_in['w1_2'], 'L0_rec_b1_2': _L0_rec_in['b1_2'], 'L0_rec_w2_2': _L0_rec_in['w2_2'], 'L0_rec_b2_2': _L0_rec_in['b2_2'], 'L0_rec_lin_w': _L0_rec_in['lin_w'], 'L0_rec_lin_b': _L0_rec_in['lin_b']}

def reference(r_x, L0_rec_emb_table, L0_rec_w1_0, L0_rec_b1_0, L0_rec_w2_0, L0_rec_b2_0, L0_rec_w1_1, L0_rec_b1_1, L0_rec_w2_1, L0_rec_b2_1, L0_rec_w1_2, L0_rec_b1_2, L0_rec_w2_2, L0_rec_b2_2, L0_rec_lin_w, L0_rec_lin_b):
    import jax
    import jax.numpy as jnp

    def _L0_rec_ref(x, emb_table, w1_0, b1_0, w2_0, b2_0, w1_1, b1_1, w2_1, b2_1, w1_2, b1_2, w2_2, b2_2, lin_w, lin_b):
        import jax, jax.numpy as jnp
        import numpy as np
        V = 125000
        D = 64
        F = 26
        L = 8
        B = 512
        IN_DIM = F * D
        HIDDENS = (1024, 1024, 512)
        pooled = emb_table[x].sum(axis=2)
        feat = pooled.reshape(x.shape[0], -1)
        for w1, b1, w2, b2 in ((w1_0, b1_0, w2_0, b2_0), (w1_1, b1_1, w2_1, b2_1), (w1_2, b1_2, w2_2, b2_2)):
            h = jax.nn.relu(feat @ w1 + b1)
            feat = jax.nn.relu(h @ w2 + b2 + feat)
        return jax.nn.sigmoid(feat @ lin_w + lin_b)
    y = _L0_rec_ref(r_x, L0_rec_emb_table, L0_rec_w1_0, L0_rec_b1_0, L0_rec_w2_0, L0_rec_b2_0, L0_rec_w1_1, L0_rec_b1_1, L0_rec_w2_1, L0_rec_b2_1, L0_rec_w1_2, L0_rec_b1_2, L0_rec_w2_2, L0_rec_b2_2, L0_rec_lin_w, L0_rec_lin_b)
    return y

_drawn_inputs = setup_inputs


def setup_inputs(seed=0):
    import zlib

    import numpy as np

    out = dict(_drawn_inputs(seed))
    spreads = {'L0_rec_b1_0': (0.0, 0.8),
     'L0_rec_b2_0': (0.0, 0.427),
     'L0_rec_b1_1': (0.0, 0.8),
     'L0_rec_b2_1': (0.0, 0.8),
     'L0_rec_b1_2': (0.0, 2.0),
     'L0_rec_b2_2': (0.0, 2.0)}
    factors = {'L0_rec_emb_table': 8.0,
     'L0_rec_w1_0': 8.0,
     'L0_rec_w2_0': 7.998,
     'L0_rec_w1_1': 8.0,
     'L0_rec_w1_2': 6.839,
     'L0_rec_w2_2': 3.446}
    for name, (base, spread) in spreads.items():
        noise = np.random.default_rng([zlib.crc32(name.encode()), seed]).standard_normal(out[name].shape)
        drawn = base * np.exp(spread * noise) if base else spread * noise
        out[name] = jnp.asarray(drawn.astype(out[name].dtype))
    for name, factor in factors.items():
        out[name] = (out[name] * factor).astype(out[name].dtype)
    return out
```

```python
import concourse.bass as bass
from concourse import mybir
from contextlib import ExitStack


def build_rec(nc, r_x, table, w1s, b1s, w2s, b2s, lin_w, lin_b, out):
    F32 = mybir.dt.float32
    ALU = mybir.AluOpType
    ACT = mybir.ActivationFunctionType
    AX_X = mybir.AxisListType.X

    P = 128
    BATCH, FIELDS, BAG = r_x.shape
    DIM = table.shape[1]
    FEATS = FIELDS * DIM
    CHUNKS = FEATS // P
    FPC = P // DIM
    BLOCKS = len(w1s)
    HC = [w.shape[1] // P for w in w1s]
    HMAX = max(HC)
    WIDE = 2
    NARROW_PASSES = 2
    WIDE_PASSES = (BATCH // P - NARROW_PASSES) // WIDE
    PASSES = WIDE_PASSES + NARROW_PASSES
    SLOTS = 13
    WSLOTS = 4
    assert FEATS % P == 0 and DIM * FPC == P and WIDE * FIELDS % SLOTS == 0 and FIELDS % SLOTS == 0
    assert WIDE_PASSES * WIDE + NARROW_PASSES == BATCH // P
    IDX_HALF = 7

    matrices = [w for pair in zip(w1s, w2s) for w in pair]
    ROWS = [w.shape[0] // P for w in matrices]
    COLS = [w.shape[1] // P for w in matrices]
    PIECES = [(i, a, b) for i in range(2 * BLOCKS)
              for a, b in ((0, (COLS[i] + 1) // 2), ((COLS[i] + 1) // 2, COLS[i]))]
    NP = len(PIECES)
    assert NP % WSLOTS == 0
    WSIZE = max(ROWS[i] * (b - a) * P for i, a, b in PIECES)

    HID = sum(HC)
    RES = BLOCKS * CHUNKS
    HID0 = [sum(HC[:i]) for i in range(BLOCKS)]
    VEC = [b.shape[0] // P for b in b1s + b2s] + [CHUNKS]
    VEC0 = [sum(VEC[:i]) for i in range(len(VEC))]
    NVEC = sum(VEC)
    VEC_DMAS = len(VEC) + 1
    OUT0 = [sum(COLS[1:i]) for i in range(2 * BLOCKS + 1)]
    HEAD_BANK = OUT0[2 * BLOCKS] % 2
    assert (OUT0[2 * BLOCKS] + 1) % 2 == 0

    def first_sample(p, units):
        return p * (WIDE * P) if units == WIDE else p * P + WIDE_PASSES * (WIDE - 1) * P

    def fields_before(p, units):
        return p * (WIDE * FIELDS) if units == WIDE else p * FIELDS + WIDE_PASSES * (WIDE - 1) * FIELDS

    def rows_before(p, units):
        per_unit = FIELDS // SLOTS * BAG * 16
        return p * (WIDE * per_unit) if units == WIDE else p * per_unit + WIDE_PASSES * (WIDE - 1) * per_unit

    def field_order(units):
        return [(g, u, f) for g in range(CHUNKS) for u in range(units) for f in range(FPC)]

    LATER = sum(r * c for r, c in list(zip(ROWS, COLS))[1:])

    def fields_due(macs, units):
        return macs * 19 * units // (2 * LATER)

    ctx = ExitStack()
    with ctx:
        def sb(name, shape, dt=F32):
            return ctx.enter_context(nc.sbuf_tensor(name, shape, dt))

        def pb(name, shape):
            return ctx.enter_context(nc.psum_tensor(name, shape, F32))

        def sem(name):
            return ctx.enter_context(nc.semaphore(name))

        weights = sb("weights", [P, WSLOTS, WSIZE])
        idx_a = sb("idx_a", [P, WIDE, IDX_HALF * FPC * BAG], r_x.dtype)
        idx_b = sb("idx_b", [P, WIDE, (CHUNKS - IDX_HALF) * FPC * BAG], r_x.dtype)
        rows = sb("rows", [P, SLOTS, BAG * DIM])
        pooled = sb("pooled", [P, CHUNKS, WIDE, P])
        feat = sb("feat", [P, CHUNKS, WIDE * P])
        hidden = sb("hidden", [P, HMAX, WIDE * P])
        presum = sb("presum", [P, 2, WIDE * P])
        ident = sb("ident", [P, P])
        vec_rows = sb("vec_rows", [NVEC, P])
        vecs = sb("vecs", [P, NVEC])
        head_bias = sb("head_bias", [1, 1])
        prob = sb("prob", [1, WIDE * P])

        BANK = 512
        PER_BANK = BANK // (WIDE * P)
        first_sum = pb("first_sum", [P, HC[0], WIDE * P])
        turned = pb("turned", [P, 2, BANK])
        sums = pb("sums", [P, 2, BANK])

        vec_rows_loaded = sem("vec_rows_loaded")
        vecs_turned = sem("vecs_turned")
        vecs_ready = sem("vecs_ready")
        ident_zeroed = sem("ident_zeroed")
        ident_ready = sem("ident_ready")
        idx_a_loaded = sem("idx_a_loaded")
        idx_b_loaded = sem("idx_b_loaded")
        rows_landed = [sem(f"rows_landed_{s}") for s in range(SLOTS)]
        fields_begun = sem("fields_begun")
        fields_pooled = sem("fields_pooled")
        chunks_turned = sem("chunks_turned")
        feat_copied = sem("feat_copied")
        weight_landed = [sem(f"weight_landed_{s}") for s in range(WSLOTS)]
        hidden_summed = sem("hidden_summed")
        hidden_ready = sem("hidden_ready")
        feat_summed = sem("feat_summed")
        residual_added = sem("residual_added")
        feat_ready = sem("feat_ready")
        logit_summed = sem("logit_summed")
        prob_ready = sem("prob_ready")
        prob_stored = sem("prob_stored")

        def block_of(j, k, m):
            _, a, b = PIECES[j]
            at = (k * (b - a) + m - a) * P
            return weights[:, j % WSLOTS, at:at + P]

        block = ctx.enter_context(nc.Block())

        @block.gpsimd
        def _(pool):
            nc.gpsimd.memset(ident[:, :], 0.0).then_inc(ident_zeroed, 1)
            pool.wait_ge(ident_zeroed, 1)
            nc.gpsimd.affine_select(out=ident[:, :], in_=ident[:, :], compare_op=ALU.not_equal,
                                    fill=1.0, base=0, pattern=[[-1, P]],
                                    channel_multiplier=1).then_inc(ident_ready, 1)

            def gather(p, units):
                for n, (g, u, f) in enumerate(field_order(units)):
                    if (g, u, f) == (0, 0, 0):
                        pool.wait_ge(idx_a_loaded, p * 16 + 16)
                    if (g, u, f) == (IDX_HALF, 0, 0):
                        pool.wait_ge(idx_b_loaded, p * 16 + 16)
                    idx, g0 = (idx_a, 0) if g < IDX_HALF else (idx_b, IDX_HALF)
                    col = ((g - g0) * FPC + f) * BAG
                    s = n % SLOTS
                    pool.wait_ge(fields_pooled, fields_before(p, units) + (n + 1))
                    pool.sem_inc(fields_begun, 1)
                    for b in range(BAG):
                        pool.indirect_dma_start(
                            out=rows[:, s, b * DIM:(b + 1) * DIM], out_offset=None, in_=table,
                            in_offset=bass.IndirectOffsetOnAxis(ap=idx[:, u, col + b:col + b + 1], axis=0),
                        ).then_inc(rows_landed[s], 16)

            with pool.Fori(0, WIDE_PASSES) as p:
                gather(p, WIDE)
            with pool.Fori(WIDE_PASSES, PASSES) as p:
                gather(p, 1)

        @block.vector
        def _(dve):
            dve.sem_inc(fields_pooled, SLOTS)

            def pool_fields(p, units, start, end):
                for n in range(start, end):
                    g, u, f = field_order(units)[n]
                    if (u, f) == (0, 0):
                        dve.wait_ge(chunks_turned, p * CHUNKS + (g + 1))
                    dve.wait_ge(rows_landed[n % SLOTS],
                                rows_before(p, units) + (n // SLOTS + 1) * BAG * 16)
                    nc.vector.tensor_reduce(
                        out=pooled[:, g, u, f * DIM:(f + 1) * DIM],
                        in_=rows[:, n % SLOTS, :].rearrange("p (b d) -> p d b", b=BAG),
                        axis=AX_X, op=ALU.add).then_inc(fields_pooled, 1)

            def one_pass(p, units, early, after, after_units):
                pool_fields(p, units, early, units * FIELDS)
                N = units * P
                macs = done = 0
                for i in range(BLOCKS):
                    if i:
                        macs += ROWS[2 * i] * COLS[2 * i]
                    for m in range(CHUNKS):
                        n = i * CHUNKS + m
                        dve.wait_ge(feat_summed, p * RES + (n + 1))
                        if n >= 2:
                            dve.wait_ge(feat_ready, p * RES + (n - 1))
                        col = VEC0[BLOCKS + i] + m
                        nc.vector.scalar_tensor_tensor(
                            out=presum[:, n % 2, 0:N], in0=sums[:, (OUT0[2 * i + 1] + m) % 2, 0:N],
                            scalar=vecs[:, col:col + 1], in1=feat[:, m, 0:N],
                            op0=ALU.add, op1=ALU.add).then_inc(residual_added, 1)
                        macs += ROWS[2 * i + 1]
                        if after is not None:
                            due = fields_due(macs, after_units)
                            pool_fields(after, after_units, done, due)
                            done = due

            dve.wait_ge(vecs_turned, 1)
            nc.vector.tensor_copy(vecs[:, :], sums[:, 0, 0:NVEC]).then_inc(vecs_ready, 1)
            dve.wait_ge(vecs_ready, 1)

            early, early_narrow = fields_due(LATER, WIDE), fields_due(LATER, 1)
            pool_fields(0, WIDE, 0, early)
            with dve.Fori(0, WIDE_PASSES - 1) as p:
                one_pass(p, WIDE, early, p + 1, WIDE)
            one_pass(WIDE_PASSES - 1, WIDE, early, WIDE_PASSES, 1)
            with dve.Fori(WIDE_PASSES, PASSES - 1) as p:
                one_pass(p, 1, early_narrow, p + 1, 1)
            one_pass(PASSES - 1, 1, early_narrow, None, None)

        @block.tensor
        def _(pe):
            pe.sem_inc(chunks_turned, CHUNKS)
            pe.wait_ge(ident_ready, 1)
            pe.wait_ge(vec_rows_loaded, VEC_DMAS * 16)
            nc.tensor.transpose(sums[:, 0, 0:NVEC], vec_rows[:, :],
                                ident[0:NVEC, 0:NVEC]).then_inc(vecs_turned, 1)
            pe.wait_ge(vecs_ready, 1)

            def piece_landed(p, j):
                pe.wait_ge(weight_landed[j % WSLOTS], p * (NP // WSLOTS * 16) + (j // WSLOTS + 1) * 16)

            def turn(p, units, k):
                pe.wait_ge(fields_pooled, fields_before(p, units) + (SLOTS + (k + 1) * units * FPC))
                for u in range(units):
                    last = nc.tensor.transpose(turned[:, k % 2, u * P:(u + 1) * P],
                                               pooled[:, k, u, :], ident[:, :])
                last.then_inc(chunks_turned, 1)

            def first_matrix(p, units):
                N = units * P
                turn(p, units, 0)
                for k in range(CHUNKS):
                    if k + 1 < CHUNKS - 1:
                        turn(p, units, k + 1)
                    if k == CHUNKS - 1:
                        turn(p, units, k)
                    pe.wait_ge(feat_copied, p * CHUNKS + (k + 1))
                    for j, (_, a, b) in enumerate(PIECES[:2]):
                        if k == 0:
                            piece_landed(p, j)
                        for m in range(a, b):
                            last = nc.tensor.matmul(
                                first_sum[:, m, 0:N], block_of(j, k, m), feat[:, k, 0:N],
                                start=(k == 0 and m % PER_BANK == 0), stop=(k == CHUNKS - 1),
                                skip_group_check=True)
                            if k == CHUNKS - 1 and m % PER_BANK == PER_BANK - 1:
                                last.then_inc(hidden_summed, PER_BANK)

            def later_matrix(p, units, i):
                N = units * P
                blk, down = i // 2, i % 2
                if down:
                    inputs, ready, before = hidden, hidden_ready, p * HID + HID0[blk]
                    own, own_before, done = residual_added, p * RES + blk * CHUNKS, feat_summed
                else:
                    inputs, ready, before = feat, feat_ready, p * RES + (blk - 1) * CHUNKS
                    own, own_before, done = hidden_ready, p * HID + HID0[blk], hidden_summed
                emptied = hidden_ready if down else residual_added
                for j, (_, a, b) in enumerate(PIECES):
                    if _ != i:
                        continue
                    piece_landed(p, j)
                    for m in range(a, b):
                        if m >= 2:
                            pe.wait_ge(own, own_before + (m - 1))
                        elif i > 1 and m == 0:
                            pe.wait_ge(emptied, before + (ROWS[i] - 1))
                        bank = (OUT0[i] + m) % 2
                        for k in range(ROWS[i]):
                            if m == 0:
                                pe.wait_ge(ready, before + (k + 1))
                            last = nc.tensor.matmul(sums[:, bank, 0:N], block_of(j, k, m),
                                                    inputs[:, k, 0:N], start=(k == 0),
                                                    stop=(k == ROWS[i] - 1))
                        last.then_inc(done, 1)

            def head(p, units):
                N = units * P
                pe.wait_ge(residual_added, p * RES + (RES - 1))
                for k in range(CHUNKS):
                    pe.wait_ge(feat_ready, p * RES + (RES - CHUNKS + k + 1))
                    col = VEC0[-1] + k
                    last = nc.tensor.matmul(sums[0:1, HEAD_BANK, 0:N], vecs[:, col:col + 1],
                                            feat[:, k, 0:N], start=(k == 0), stop=(k == CHUNKS - 1))
                last.then_inc(logit_summed, 1)

            def one_pass(p, units):
                first_matrix(p, units)
                for i in range(1, 2 * BLOCKS):
                    later_matrix(p, units, i)
                head(p, units)

            with pe.Fori(0, WIDE_PASSES) as p:
                one_pass(p, WIDE)
            with pe.Fori(WIDE_PASSES, PASSES) as p:
                one_pass(p, 1)

        @block.scalar
        def _(act):
            for n, v in enumerate(b1s + b2s + [lin_w.rearrange("n o -> (n o)")]):
                act.dma_start(vec_rows[VEC0[n]:VEC0[n] + VEC[n], :],
                              v.rearrange("(k p) -> k p", p=P)).then_inc(vec_rows_loaded, 16)
            act.dma_start(head_bias[:, :], lin_b.rearrange("(a b) -> a b", a=1)).then_inc(vec_rows_loaded, 16)
            act.wait_ge(vec_rows_loaded, VEC_DMAS * 16)
            act.wait_ge(vecs_ready, 1)

            def relus(p, units, i):
                N = units * P
                blk, down = i // 2, i % 2
                for m in range(COLS[i]):
                    if down:
                        n = blk * CHUNKS + m
                        act.wait_ge(residual_added, p * RES + (n + 1))
                        nc.scalar.activation(feat[:, m, 0:N], presum[:, n % 2, 0:N],
                                             ACT.Relu).then_inc(feat_ready, 1)
                    else:
                        act.wait_ge(hidden_summed, p * HID + (HID0[blk] + m + 1))
                        source = sums[:, (OUT0[i] + m) % 2, 0:N] if i else first_sum[:, m, 0:N]
                        col = VEC0[blk] + m
                        nc.scalar.activation(hidden[:, m, 0:N], source, ACT.Relu,
                                             bias=vecs[:, col:col + 1]).then_inc(hidden_ready, 1)

            def one_pass(p, units):
                N = units * P
                for k in range(CHUNKS):
                    act.wait_ge(chunks_turned, p * CHUNKS + (CHUNKS + k + 1))
                    nc.scalar.copy(feat[:, k, 0:N], turned[:, k % 2, 0:N]).then_inc(feat_copied, 1)
                for i in range(2 * BLOCKS):
                    relus(p, units, i)
                act.wait_ge(logit_summed, p + 1)
                nc.scalar.activation(prob[:, 0:N], sums[0:1, HEAD_BANK, 0:N], ACT.Sigmoid,
                                     bias=head_bias[:, :]).then_inc(prob_ready, 1)
                act.wait_ge(prob_ready, p + 1)
                act.dma_start(out.rearrange("n o -> o n")[:, bass.ds(first_sample(p, units), N)],
                              prob[:, 0:N]).then_inc(prob_stored, 16)
                act.wait_ge(prob_stored, p * 16 + 16)

            with act.Fori(0, WIDE_PASSES) as p:
                one_pass(p, WIDE)
            with act.Fori(WIDE_PASSES, PASSES) as p:
                one_pass(p, 1)

        @block.sync
        def _(sp):
            def load_idx(p, units, part):
                tile, done, g0, g1 = ((idx_a, idx_a_loaded, 0, IDX_HALF),
                                      (idx_b, idx_b_loaded, IDX_HALF, CHUNKS))[part]
                src = r_x.rearrange("n f b -> n (f b)")[bass.ds(first_sample(p, units), units * P),
                                                        g0 * FPC * BAG:g1 * FPC * BAG]
                sp.dma_start(tile[:, 0:units, :],
                             src.rearrange("(u s) c -> s u c", s=P)).then_inc(done, 16)

            def load_piece(j):
                i, a, b = PIECES[j]
                n = ROWS[i] * (b - a) * P
                sp.dma_start(weights[:, j % WSLOTS, 0:n].rearrange("p (k c) -> p k c", k=ROWS[i]),
                             matrices[i].rearrange("(k p) c -> p k c", p=P)[:, :, a * P:b * P]
                             ).then_inc(weight_landed[j % WSLOTS], 16)

            def piece_used(p, j):
                i, _, b = PIECES[j]
                if i % 2:
                    sp.wait_ge(feat_summed, p * RES + (i // 2 * CHUNKS + b))
                else:
                    sp.wait_ge(hidden_summed, p * HID + (HID0[i // 2] + b))

            def one_pass(p, units, after, after_units):
                if after is not None:
                    sp.wait_ge(fields_pooled,
                               fields_before(p, units) + (SLOTS + IDX_HALF * units * FPC))
                    load_idx(after, after_units, 0)
                for j in range(NP):
                    if j == 1 and after is not None:
                        sp.wait_ge(fields_pooled, fields_before(p, units) + (SLOTS + units * FIELDS))
                        load_idx(after, after_units, 1)
                    if j + WSLOTS < NP or after is not None:
                        piece_used(p, j)
                        load_piece((j + WSLOTS) % NP)

            load_idx(0, WIDE, 0)
            load_idx(0, WIDE, 1)
            for j in range(WSLOTS):
                load_piece(j)
            with sp.Fori(0, WIDE_PASSES - 1) as p:
                one_pass(p, WIDE, p + 1, WIDE)
            one_pass(WIDE_PASSES - 1, WIDE, WIDE_PASSES, 1)
            with sp.Fori(WIDE_PASSES, PASSES - 1) as p:
                one_pass(p, 1, p + 1, 1)
            one_pass(PASSES - 1, 1, None, None)


_INS = ["r_x", "emb_table", "w1_0", "b1_0", "w2_0", "b2_0", "w1_1", "b1_1", "w2_1", "b2_1",
        "w1_2", "b1_2", "w2_2", "b2_2", "lin_w", "lin_b"]


def kernel(**inputs):
    import numpy as np
    import concourse.bacc as bacc
    from concourse.bass_utils import run_bass_kernel_spmd

    nc = bacc.Bacc("TRN2", target_bir_lowering=False, num_devices=1)
    arrays, aps = {}, {}
    for name in _INS:
        a = np.ascontiguousarray(inputs[name if name == "r_x" else f"L0_rec_{name}"])
        arrays[f"in_{name}"] = a
        aps[name] = nc.dram_tensor(f"in_{name}", a.shape, mybir.dt.from_np(a.dtype),
                                   kind="ExternalInput").ap()
    out = nc.dram_tensor("out_0", (arrays["in_r_x"].shape[0], 1), mybir.dt.float32,
                         kind="ExternalOutput").ap()
    build_rec(nc, aps["r_x"], aps["emb_table"],
              [aps[f"w1_{i}"] for i in range(3)], [aps[f"b1_{i}"] for i in range(3)],
              [aps[f"w2_{i}"] for i in range(3)], [aps[f"b2_{i}"] for i in range(3)],
              aps["lin_w"], aps["lin_b"], out)
    return run_bass_kernel_spmd(nc, [arrays], core_ids=[0]).results[0]["out_0"]
```

```python
import concourse.bass as bass
from concourse import mybir
from contextlib import ExitStack


def build_rec(nc, r_x, table, w1s, b1s, w2s, b2s, lin_w, lin_b, out):
    F32 = mybir.dt.float32
    ALU = mybir.AluOpType
    ACT = mybir.ActivationFunctionType
    AX_X = mybir.AxisListType.X

    P = 128
    BATCH, FIELDS, BAG = r_x.shape
    DIM = table.shape[1]
    FEATS = FIELDS * DIM
    CHUNKS = FEATS // P
    FPC = P // DIM
    BLOCKS = len(w1s)
    HC = [w.shape[1] // P for w in w1s]
    HMAX = max(HC)
    WIDE = 2
    NARROW_PASSES = 2
    WIDE_PASSES = (BATCH // P - NARROW_PASSES) // WIDE
    PASSES = WIDE_PASSES + NARROW_PASSES
    SLOTS = 13
    WSLOTS = 4
    assert FEATS % P == 0 and DIM * FPC == P and WIDE * FIELDS % SLOTS == 0 and FIELDS % SLOTS == 0
    assert WIDE_PASSES * WIDE + NARROW_PASSES == BATCH // P
    IDX_HALF = 7

    matrices = [w for pair in zip(w1s, w2s) for w in pair]
    ROWS = [w.shape[0] // P for w in matrices]
    COLS = [w.shape[1] // P for w in matrices]
    PIECES = []
    for i, (rs, cs) in enumerate(zip(ROWS, COLS)):
        r_cut, c_cut = (rs + 1) // 2, (cs + 1) // 2
        PIECES += ([(i, 0, r_cut, 0, cs), (i, r_cut, rs, 0, cs)] if i == 0 else
                   [(i, 0, rs, 0, c_cut), (i, 0, rs, c_cut, cs)])
    PIECE_COUNT = len(PIECES)
    assert PIECE_COUNT % WSLOTS == 0
    WSIZE = max((r1 - r0) * (c1 - c0) * P for _, r0, r1, c0, c1 in PIECES)

    HID = sum(HC)
    RES = BLOCKS * CHUNKS
    HID0 = [sum(HC[:i]) for i in range(BLOCKS)]
    VEC = [b.shape[0] // P for b in b1s + b2s] + [CHUNKS]
    VEC0 = [sum(VEC[:i]) for i in range(len(VEC))]
    NVEC = sum(VEC)
    VEC_DMAS = len(VEC) + 1
    OUT0 = [sum(COLS[1:i]) for i in range(2 * BLOCKS)]

    def first_sample(p, units):
        return p * (WIDE * P) if units == WIDE else p * P + WIDE_PASSES * (WIDE - 1) * P

    def fields_before(p, units):
        return p * (WIDE * FIELDS) if units == WIDE else p * FIELDS + WIDE_PASSES * (WIDE - 1) * FIELDS

    def rows_before(p, units):
        per_unit = FIELDS // SLOTS * BAG * 16
        return p * (WIDE * per_unit) if units == WIDE else p * per_unit + WIDE_PASSES * (WIDE - 1) * per_unit

    def field_order(units):
        return [(g, u, f) for g in range(CHUNKS) for u in range(units) for f in range(FPC)]

    LATER = sum(r * c for r, c in list(zip(ROWS, COLS))[1:])

    def fields_due(blocks, units):
        return blocks * 19 * units // (WIDE * LATER)

    ctx = ExitStack()
    with ctx:
        def sb(name, shape, dt=F32):
            return ctx.enter_context(nc.sbuf_tensor(name, shape, dt))

        def pb(name, shape):
            return ctx.enter_context(nc.psum_tensor(name, shape, F32))

        def sem(name):
            return ctx.enter_context(nc.semaphore(name))

        weights = sb("weights", [P, WSLOTS, WSIZE])
        idx_a = sb("idx_a", [P, WIDE, IDX_HALF * FPC * BAG], r_x.dtype)
        idx_b = sb("idx_b", [P, WIDE, (CHUNKS - IDX_HALF) * FPC * BAG], r_x.dtype)
        rows = sb("rows", [P, SLOTS, BAG * DIM])
        pooled = sb("pooled", [P, CHUNKS, WIDE, P])
        feat = sb("feat", [P, CHUNKS, WIDE * P])
        hidden = sb("hidden", [P, HMAX, WIDE * P])
        presum = sb("presum", [P, 2, WIDE * P])
        ident = sb("ident", [P, P])
        vec_rows = sb("vec_rows", [NVEC, P])
        vecs = sb("vecs", [P, NVEC])
        head_bias = sb("head_bias", [1, 1])
        prob = sb("prob", [1, WIDE * P])

        BANK = 512
        PER_BANK = BANK // (WIDE * P)
        first_sum = pb("first_sum", [P, HC[0], WIDE * P])
        turned = pb("turned", [P, 2, BANK])
        sums = pb("sums", [P, 2, BANK])

        vec_rows_loaded = sem("vec_rows_loaded")
        vecs_turned = sem("vecs_turned")
        vecs_ready = sem("vecs_ready")
        ident_zeroed = sem("ident_zeroed")
        ident_ready = sem("ident_ready")
        idx_a_loaded = sem("idx_a_loaded")
        idx_b_loaded = sem("idx_b_loaded")
        rows_landed = [sem(f"rows_landed_{s}") for s in range(SLOTS)]
        fields_begun = sem("fields_begun")
        fields_pooled = sem("fields_pooled")
        chunks_turned = sem("chunks_turned")
        feat_copied = sem("feat_copied")
        weight_landed = [sem(f"weight_landed_{s}") for s in range(WSLOTS)]
        first_piece_used = sem("first_piece_used")
        hidden_summed = sem("hidden_summed")
        hidden_ready = sem("hidden_ready")
        feat_summed = sem("feat_summed")
        residual_added = sem("residual_added")
        feat_ready = sem("feat_ready")
        logit_summed = sem("logit_summed")
        prob_ready = sem("prob_ready")
        prob_stored = sem("prob_stored")

        def block_of(j, k, m):
            _, r0, _, c0, c1 = PIECES[j]
            at = ((k - r0) * (c1 - c0) + m - c0) * P
            return weights[:, j % WSLOTS, at:at + P]

        block = ctx.enter_context(nc.Block())

        @block.gpsimd
        def _(pool):
            nc.gpsimd.memset(ident[:, :], 0.0).then_inc(ident_zeroed, 1)
            pool.wait_ge(ident_zeroed, 1)
            nc.gpsimd.affine_select(out=ident[:, :], in_=ident[:, :], compare_op=ALU.not_equal,
                                    fill=1.0, base=0, pattern=[[-1, P]],
                                    channel_multiplier=1).then_inc(ident_ready, 1)

            def gather(p, units):
                for n, (g, u, f) in enumerate(field_order(units)):
                    if (g, u, f) == (0, 0, 0):
                        pool.wait_ge(idx_a_loaded, p * 16 + 16)
                    if (g, u, f) == (IDX_HALF, 0, 0):
                        pool.wait_ge(idx_b_loaded, p * 16 + 16)
                    idx, g0 = (idx_a, 0) if g < IDX_HALF else (idx_b, IDX_HALF)
                    col = ((g - g0) * FPC + f) * BAG
                    s = n % SLOTS
                    pool.wait_ge(fields_pooled, fields_before(p, units) + (n + 1))
                    pool.sem_inc(fields_begun, 1)
                    for b in range(BAG):
                        pool.indirect_dma_start(
                            out=rows[:, s, b * DIM:(b + 1) * DIM], out_offset=None, in_=table,
                            in_offset=bass.IndirectOffsetOnAxis(ap=idx[:, u, col + b:col + b + 1], axis=0),
                        ).then_inc(rows_landed[s], 16)

            with pool.Fori(0, WIDE_PASSES) as p:
                gather(p, WIDE)
            with pool.Fori(WIDE_PASSES, PASSES) as p:
                gather(p, 1)

        @block.vector
        def _(dve):
            dve.sem_inc(fields_pooled, SLOTS)

            def pool_fields(p, units, start, end):
                for n in range(start, end):
                    g, u, f = field_order(units)[n]
                    if (u, f) == (0, 0):
                        dve.wait_ge(chunks_turned, p * CHUNKS + (g + 1))
                    dve.wait_ge(rows_landed[n % SLOTS],
                                rows_before(p, units) + (n // SLOTS + 1) * BAG * 16)
                    nc.vector.tensor_reduce(
                        out=pooled[:, g, u, f * DIM:(f + 1) * DIM],
                        in_=rows[:, n % SLOTS, :].rearrange("p (b d) -> p d b", b=BAG),
                        axis=AX_X, op=ALU.add).then_inc(fields_pooled, 1)

            def one_pass(p, units, early, after, after_units):
                pool_fields(p, units, early, units * FIELDS)
                N = units * P
                blocks = done = 0
                for i in range(BLOCKS):
                    if i:
                        blocks += ROWS[2 * i] * COLS[2 * i]
                    for m in range(CHUNKS):
                        n = i * CHUNKS + m
                        dve.wait_ge(feat_summed, p * RES + (n + 1))
                        if n >= 2:
                            dve.wait_ge(feat_ready, p * RES + (n - 1))
                        col = VEC0[BLOCKS + i] + m
                        nc.vector.scalar_tensor_tensor(
                            out=presum[:, n % 2, 0:N], in0=sums[:, (OUT0[2 * i + 1] + m) % 2, 0:N],
                            scalar=vecs[:, col:col + 1], in1=feat[:, m, 0:N],
                            op0=ALU.add, op1=ALU.add).then_inc(residual_added, 1)
                        blocks += ROWS[2 * i + 1]
                        if after is not None:
                            due = fields_due(blocks, units)
                            pool_fields(after, after_units, done, due)
                            done = due

            dve.wait_ge(vecs_turned, 1)
            nc.vector.tensor_copy(vecs[:, :], sums[:, 0, 0:NVEC]).then_inc(vecs_ready, 1)
            dve.wait_ge(vecs_ready, 1)

            early, early_narrow = fields_due(LATER, WIDE), fields_due(LATER, 1)
            pool_fields(0, WIDE, 0, early)
            with dve.Fori(0, WIDE_PASSES - 1) as p:
                one_pass(p, WIDE, early, p + 1, WIDE)
            one_pass(WIDE_PASSES - 1, WIDE, early, WIDE_PASSES, 1)
            assert NARROW_PASSES == 2
            one_pass(PASSES - 2, 1, early, PASSES - 1, 1)
            one_pass(PASSES - 1, 1, early_narrow, None, None)

        @block.tensor
        def _(pe):
            pe.sem_inc(chunks_turned, CHUNKS)
            pe.wait_ge(ident_ready, 1)
            pe.wait_ge(vec_rows_loaded, VEC_DMAS * 16)
            nc.tensor.transpose(sums[:, 0, 0:NVEC], vec_rows[:, :],
                                ident[0:NVEC, 0:NVEC]).then_inc(vecs_turned, 1)
            pe.wait_ge(vecs_ready, 1)

            def piece_landed(p, j):
                pe.wait_ge(weight_landed[j % WSLOTS], p * (PIECE_COUNT // WSLOTS * 16) + (j // WSLOTS + 1) * 16)

            def turn(p, units, k):
                pe.wait_ge(fields_pooled, fields_before(p, units) + (SLOTS + (k + 1) * units * FPC))
                for u in range(units):
                    last = nc.tensor.transpose(turned[:, k % 2, u * P:(u + 1) * P],
                                               pooled[:, k, u, :], ident[:, :])
                last.then_inc(chunks_turned, 1)

            def first_matrix(p, units):
                N = units * P
                turn(p, units, 0)
                for k in range(CHUNKS):
                    if k + 1 < CHUNKS - 1:
                        turn(p, units, k + 1)
                    if k == CHUNKS - 1:
                        turn(p, units, k)
                    pe.wait_ge(feat_copied, p * CHUNKS + (k + 1))
                    j = 0 if k < PIECES[1][1] else 1
                    if k == PIECES[j][1]:
                        piece_landed(p, j)
                    for m in range(HC[0]):
                        last = nc.tensor.matmul(
                            first_sum[:, m, 0:N], block_of(j, k, m), feat[:, k, 0:N],
                            start=(k == 0 and m % PER_BANK == 0), stop=(k == CHUNKS - 1),
                            skip_group_check=True)
                        if k == CHUNKS - 1 and m % PER_BANK == PER_BANK - 1:
                            last.then_inc(hidden_summed, PER_BANK)
                    if k == PIECES[0][2] - 1:
                        last.then_inc(first_piece_used, 1)

            def later_matrix(p, units, i):
                N = units * P
                blk, down = i // 2, i % 2
                if down:
                    inputs, ready, before = hidden, hidden_ready, p * HID + HID0[blk]
                    own, own_before, done = residual_added, p * RES + blk * CHUNKS, feat_summed
                else:
                    inputs, ready, before = feat, feat_ready, p * RES + (blk - 1) * CHUNKS
                    own, own_before, done = hidden_ready, p * HID + HID0[blk], hidden_summed
                emptied = hidden_ready if down else residual_added
                for j in (2 * i, 2 * i + 1):
                    piece_landed(p, j)
                    for m in range(PIECES[j][3], PIECES[j][4]):
                        if m >= 2:
                            pe.wait_ge(own, own_before + (m - 1))
                        elif i > 1 and m == 0:
                            pe.wait_ge(emptied, before + (ROWS[i] - 1))
                        bank = (OUT0[i] + m) % 2
                        for k in range(ROWS[i]):
                            if m == 0:
                                pe.wait_ge(ready, before + (k + 1))
                            last = nc.tensor.matmul(sums[:, bank, 0:N], block_of(j, k, m),
                                                    inputs[:, k, 0:N], start=(k == 0),
                                                    stop=(k == ROWS[i] - 1))
                        last.then_inc(done, 1)
                        if i == 2 * BLOCKS - 1 and m >= HEAD_LAG:
                            head(p, units, m - HEAD_LAG)

            HEAD_LAG = 2

            def head(p, units, k):
                N = units * P
                pe.wait_ge(feat_ready, p * RES + (RES - CHUNKS + k + 1))
                col = VEC0[-1] + k
                last = nc.tensor.matmul(first_sum[0:1, 0, 0:N], vecs[:, col:col + 1],
                                        feat[:, k, 0:N], start=(k == 0), stop=(k == CHUNKS - 1))
                if k == CHUNKS - 1:
                    last.then_inc(logit_summed, 1)

            def one_pass(p, units):
                first_matrix(p, units)
                for i in range(1, 2 * BLOCKS):
                    later_matrix(p, units, i)
                for k in range(CHUNKS - HEAD_LAG, CHUNKS):
                    head(p, units, k)

            with pe.Fori(0, WIDE_PASSES) as p:
                one_pass(p, WIDE)
            with pe.Fori(WIDE_PASSES, PASSES) as p:
                one_pass(p, 1)

        @block.scalar
        def _(act):
            for n, v in enumerate(b1s + b2s + [lin_w.rearrange("n o -> (n o)")]):
                act.dma_start(vec_rows[VEC0[n]:VEC0[n] + VEC[n], :],
                              v.rearrange("(k p) -> k p", p=P)).then_inc(vec_rows_loaded, 16)
            act.dma_start(head_bias[:, :], lin_b.rearrange("(a b) -> a b", a=1)).then_inc(vec_rows_loaded, 16)
            act.wait_ge(vec_rows_loaded, VEC_DMAS * 16)
            act.wait_ge(vecs_ready, 1)

            def relus(p, units, i):
                N = units * P
                blk, down = i // 2, i % 2
                for m in range(COLS[i]):
                    if down:
                        n = blk * CHUNKS + m
                        act.wait_ge(residual_added, p * RES + (n + 1))
                        nc.scalar.activation(feat[:, m, 0:N], presum[:, n % 2, 0:N],
                                             ACT.Relu).then_inc(feat_ready, 1)
                    else:
                        act.wait_ge(hidden_summed, p * HID + (HID0[blk] + m + 1))
                        source = sums[:, (OUT0[i] + m) % 2, 0:N] if i else first_sum[:, m, 0:N]
                        col = VEC0[blk] + m
                        nc.scalar.activation(hidden[:, m, 0:N], source, ACT.Relu,
                                             bias=vecs[:, col:col + 1]).then_inc(hidden_ready, 1)

            def one_pass(p, units):
                N = units * P
                for k in range(CHUNKS):
                    act.wait_ge(chunks_turned, p * CHUNKS + (CHUNKS + k + 1))
                    nc.scalar.copy(feat[:, k, 0:N], turned[:, k % 2, 0:N]).then_inc(feat_copied, 1)
                for i in range(2 * BLOCKS):
                    relus(p, units, i)
                act.wait_ge(logit_summed, p + 1)
                nc.scalar.activation(prob[:, 0:N], first_sum[0:1, 0, 0:N], ACT.Sigmoid,
                                     bias=head_bias[:, :]).then_inc(prob_ready, 1)
                act.wait_ge(prob_ready, p + 1)
                act.dma_start(out.rearrange("n o -> o n")[:, bass.ds(first_sample(p, units), N)],
                              prob[:, 0:N]).then_inc(prob_stored, 16)
                act.wait_ge(prob_stored, p * 16 + 16)

            with act.Fori(0, WIDE_PASSES) as p:
                one_pass(p, WIDE)
            with act.Fori(WIDE_PASSES, PASSES) as p:
                one_pass(p, 1)

        @block.sync
        def _(sp):
            def load_idx(p, units, part):
                tile, done, g0, g1 = ((idx_a, idx_a_loaded, 0, IDX_HALF),
                                      (idx_b, idx_b_loaded, IDX_HALF, CHUNKS))[part]
                src = r_x.rearrange("n f b -> n (f b)")[bass.ds(first_sample(p, units), units * P),
                                                        g0 * FPC * BAG:g1 * FPC * BAG]
                sp.dma_start(tile[:, 0:units, :],
                             src.rearrange("(u s) c -> s u c", s=P)).then_inc(done, 16)

            def load_piece(j):
                i, r0, r1, c0, c1 = PIECES[j]
                to = weights[:, j % WSLOTS, 0:(r1 - r0) * (c1 - c0) * P]
                sp.dma_start(to.rearrange("p (k c) -> p k c", k=r1 - r0),
                             matrices[i].rearrange("(k p) c -> p k c", p=P)[:, r0:r1, c0 * P:c1 * P]
                             ).then_inc(weight_landed[j % WSLOTS], 16)

            def piece_used(p, j):
                i, c1 = PIECES[j][0], PIECES[j][4]
                if j == 0:
                    sp.wait_ge(first_piece_used, p + 1)
                elif i % 2:
                    sp.wait_ge(feat_summed, p * RES + (i // 2 * CHUNKS + c1))
                else:
                    sp.wait_ge(hidden_summed, p * HID + (HID0[i // 2] + c1))

            def one_pass(p, units, after, after_units):
                if after is not None:
                    sp.wait_ge(fields_pooled,
                               fields_before(p, units) + (SLOTS + IDX_HALF * units * FPC))
                    load_idx(after, after_units, 0)
                for j in range(PIECE_COUNT):
                    if j == 1 and after is not None:
                        sp.wait_ge(fields_pooled, fields_before(p, units) + (SLOTS + units * FIELDS))
                        load_idx(after, after_units, 1)
                    if j + WSLOTS < PIECE_COUNT or after is not None:
                        piece_used(p, j)
                        load_piece((j + WSLOTS) % PIECE_COUNT)

            load_idx(0, WIDE, 0)
            load_idx(0, WIDE, 1)
            for j in range(WSLOTS):
                load_piece(j)
            with sp.Fori(0, WIDE_PASSES - 1) as p:
                one_pass(p, WIDE, p + 1, WIDE)
            one_pass(WIDE_PASSES - 1, WIDE, WIDE_PASSES, 1)
            with sp.Fori(WIDE_PASSES, PASSES - 1) as p:
                one_pass(p, 1, p + 1, 1)
            one_pass(PASSES - 1, 1, None, None)


_INS = ["r_x", "emb_table", "w1_0", "b1_0", "w2_0", "b2_0", "w1_1", "b1_1", "w2_1", "b2_1",
        "w1_2", "b1_2", "w2_2", "b2_2", "lin_w", "lin_b"]


def kernel(**inputs):
    import numpy as np
    import concourse.bacc as bacc
    from concourse.bass_utils import run_bass_kernel_spmd

    nc = bacc.Bacc("TRN2", target_bir_lowering=False, num_devices=1)
    arrays, aps = {}, {}
    for name in _INS:
        a = np.ascontiguousarray(inputs[name if name == "r_x" else f"L0_rec_{name}"])
        arrays[f"in_{name}"] = a
        aps[name] = nc.dram_tensor(f"in_{name}", a.shape, mybir.dt.from_np(a.dtype),
                                   kind="ExternalInput").ap()
    out = nc.dram_tensor("out_0", (arrays["in_r_x"].shape[0], 1), mybir.dt.float32,
                         kind="ExternalOutput").ap()
    build_rec(nc, aps["r_x"], aps["emb_table"],
              [aps[f"w1_{i}"] for i in range(3)], [aps[f"b1_{i}"] for i in range(3)],
              [aps[f"w2_{i}"] for i in range(3)], [aps[f"b2_{i}"] for i in range(3)],
              aps["lin_w"], aps["lin_b"], out)
    return run_bass_kernel_spmd(nc, [arrays], core_ids=[0]).results[0]["out_0"]
```
